# Optimizing a Trainium2 kernel written in Bass

```python
import numpy as np
import jax
import jax.numpy as jnp

def _softmax(x, axis=-1):
    return jax.nn.softmax(x, axis=axis)

def _gelu(x):
    return jax.nn.gelu(x, approximate=True)

def _silu(x):
    return jax.nn.silu(x)

def _sigmoid(x):
    return jax.nn.sigmoid(x)

def _layernorm(x, axis=-1, eps=1e-05):
    m = jnp.mean(x, axis=axis, keepdims=True)
    v = jnp.var(x, axis=axis, keepdims=True)
    return (x - m) / jnp.sqrt(v + eps)

def _scatter_add(tgt, idx, src, axis=0):
    return tgt.at[idx].add(src)

def _segment_sum(src, seg, n):
    return jax.ops.segment_sum(src, seg, n)
kernel_name = 'mk_adj_resnorm_d1_adj_r2_f399a7'

def setup_inputs(seed: int=0):
    np.random.seed(seed)
    _w = jnp.asarray

    def _rec_inputs():
        import jax
        import jax.numpy as jnp
        _gk = jax.random.key(seed)
        x = -0.0002928 + 1 * jax.random.normal(jax.random.fold_in(_gk, 1), (128, 128, 1024), jnp.float32)
        _w = (1.0 + jnp.arange(128, dtype=jnp.float32)) ** (-0.5)
        _w = _w / _w.mean()
        _pij = jnp.clip(0.125 * _w[:, None] * _w[None, :], 0.0, 1.0)
        _a = jax.random.uniform(jax.random.fold_in(_gk, 2), (128, 128)) < _pij
        _a = jnp.logical_or(_a, jnp.swapaxes(_a, -1, -2))
        _a = jnp.logical_or(_a, jnp.eye(128, dtype=bool))
        _af = _a.astype(jnp.float32)
        _af = _af * jax.random.uniform(jax.random.fold_in(_gk, 3), (128, 128), jnp.float32, 0.05, 0.203735)
        adj = _af
        return (x, adj)
    x, adj = _rec_inputs()

    def _L0_gnn_setup():
        import jax, jax.numpy as jnp
        import numpy as np
        B, C, N = (16, 128, 1024)
        key = jax.random.key(seed)
        ks = jax.random.split(key, 6)
        x = jax.random.normal(ks[0], (B, C, N), jnp.float32)
        wq = jax.random.normal(ks[1], (C // 4, C), jnp.float32) * 0.05
        wv = jax.random.normal(ks[2], (C, C), jnp.float32) * 0.05
        bv = jax.random.normal(ks[3], (C,), jnp.float32) * 0.05
        wt = jax.random.normal(ks[4], (C, C), jnp.float32) * 0.05
        bt = jax.random.normal(ks[5], (C,), jnp.float32) * 0.05
        gamma = jnp.ones((C,), jnp.float32)
        beta = jnp.zeros((C,), jnp.float32)
        bn_mean = jnp.zeros((C,), jnp.float32)
        bn_var = jnp.ones((C,), jnp.float32)
        return dict(x=x, wq=wq, wv=wv, bv=bv, wt=wt, bt=bt, gamma=gamma, beta=beta, bn_mean=bn_mean, bn_var=bn_var)
    _L0_gnn_all = _L0_gnn_setup()
    _L0_gnn_in = {k: v for k, v in _L0_gnn_all.items() if k in ('wq', 'bv', 'bt', 'gamma', 'beta', 'bn_mean', 'bn_var')}
    del _L0_gnn_all
    return {'x': x, 'adj': adj, 'L0_gnn_wq': _L0_gnn_in['wq'], 'L0_gnn_bv': _L0_gnn_in['bv'], 'L0_gnn_bt': _L0_gnn_in['bt'], 'L0_gnn_gamma': _L0_gnn_in['gamma'], 'L0_gnn_beta': _L0_gnn_in['beta'], 'L0_gnn_bn_mean': _L0_gnn_in['bn_mean'], 'L0_gnn_bn_var': _L0_gnn_in['bn_var']}

def reference(x, adj, L0_gnn_wq, L0_gnn_bv, L0_gnn_bt, L0_gnn_gamma, L0_gnn_beta, L0_gnn_bn_mean, L0_gnn_bn_var):
    import jax
    import jax.numpy as jnp

    def _L0_gnn_ref(x, wq, wv, bv, wt, bt, gamma, beta, bn_mean, bn_var):
        import jax, jax.numpy as jnp
        import numpy as np
        B, C, N = (16, 128, 1024)
        EPS = 1e-09
        BN_EPS = 1e-05
        x_q = jnp.einsum('dc,bcn->bnd', wq, x)
        x_k = jnp.einsum('dc,bcn->bdn', wq, x)
        energy = jnp.einsum('bnd,bdm->bnm', x_q, x_k)
        attn = jax.nn.softmax(energy, axis=-1)
        attn = attn / (EPS + attn.sum(axis=1, keepdims=True))
        x_v = jnp.einsum('dc,bcn->bdn', wv, x) + bv[None, :, None]
        x_r = jnp.einsum('bdn,bnm->bdm', x_v, attn)
        t = jnp.einsum('dc,bcn->bdn', wt, x - x_r) + bt[None, :, None]
        t = (t - bn_mean[None, :, None]) * jax.lax.rsqrt(bn_var + BN_EPS)[None, :, None]
        t = t * gamma[None, :, None] + beta[None, :, None]
        return x + jax.nn.relu(t)
    x = _layernorm(x + _L0_gnn_ref(x, L0_gnn_wq, adj, L0_gnn_bv, adj, L0_gnn_bt, L0_gnn_gamma, L0_gnn_beta, L0_gnn_bn_mean, L0_gnn_bn_var), axis=-1)
    return x

_drawn_inputs = setup_inputs


def setup_inputs(seed=0):
    import zlib

    import numpy as np

    out = dict(_drawn_inputs(seed))
    spreads = {'L0_gnn_gamma': (1.0, 0.2),
     'L0_gnn_beta': (0.0, 0.331),
     'L0_gnn_bn_mean': (0.0, 0.316),
     'L0_gnn_bn_var': (1.0, 0.536)}
    factors = {'L0_gnn_bv': 6.678, 'L0_gnn_bt': 3.99}
    for name, (base, spread) in spreads.items():
        noise = np.random.default_rng([zlib.crc32(name.encode()), seed]).standard_normal(out[name].shape)
        drawn = base * np.exp(spread * noise) if base else spread * noise
        out[name] = jnp.asarray(drawn.astype(out[name].dtype))
    for name, factor in factors.items():
        out[name] = (out[name] * factor).astype(out[name].dtype)
    return out
```

```python
from contextlib import ExitStack

import concourse.bass as bass
from concourse import mybir

F32 = mybir.dt.float32
F32R = mybir.dt.float32r
ALU = mybir.AluOpType
ACT = mybir.ActivationFunctionType
AX = mybir.AxisListType

P = 128
BANK = 512
EPS_COL = 1e-9
EPS_BN = 1e-5
EPS_LN = 1e-5
XSLOTS = 4
UNROLL = 4
BEHIND, AHEAD, LOADED = 1, 2, 3


def attention_kernel(nc, x, adj, wq, bv, bt, gamma, beta, bn_mean, bn_var, out):
    B, C, N = x.shape
    D = wq.shape[0]
    NB = N // P
    REP = 3 * D
    VW = C + 2
    RECIP_GROUPS = [(0, 4), (4, 6), (6, 8)]
    OUT_GROUPS = [(0, 3), (3, 6), (6, 8)]
    NR, NO = len(RECIP_GROUPS), len(OUT_GROUPS)
    assert C == P and N == 2 * BANK and NB == 8 and B % UNROLL == 0 and REP <= P

    with ExitStack() as ctx:
        def sb(name, shape, dt=F32):
            return ctx.enter_context(nc.sbuf_tensor(name, shape, dt))

        def sem(name):
            return ctx.enter_context(nc.semaphore(name))

        adj_sb = sb("adj_sb", [P, C])
        wq_rep = sb("wq_rep", [REP, C])
        vec = sb("vec", [P, 6])
        zeros = sb("zeros", [P, P])
        ident = sb("ident", [P, P])
        minus_half = sb("minus_half", [P, 1])
        bn_veps = sb("bn_veps", [P, 1])
        bn_inv = sb("bn_inv", [P, 1])
        bn_scale = sb("bn_scale", [P, 1])
        bn_diff = sb("bn_diff", [P, 1])
        bn_part = sb("bn_part", [P, 1])
        bn_shift = sb("bn_shift", [P, 1])
        adj_scaled = sb("adj_scaled", [P, C])
        adj_sT = sb("adj_sT", [P, C])
        adj_sT_neg = sb("adj_sT_neg", [P, C])
        bv_cols = sb("bv_cols", [P, P])
        wq_hi = sb("wq_hi", [P, REP], F32R)
        wq_lo = sb("wq_lo", [P, REP], F32R)
        w_hi = sb("w_hi", [P, 2 * C], F32R)
        w_lo = sb("w_lo", [P, 2 * C], F32R)
        bias_pick = sb("bias_pick", [P, P], F32R)
        bias_rows = sb("bias_rows", [P, C], F32R)

        x_sb = sb("x_sb", [P, XSLOTS, N])
        x_hi = sb("x_hi", [P, 2, N], F32R)
        x_lo = sb("x_lo", [P, 2, N], F32R)
        qa = sb("qa", [REP, 2, N], F32R)
        qb = sb("qb", [REP, 2, N], F32R)
        neg_max = sb("neg_max", [P, 2, NB])
        row_sum = sb("row_sum", [P, 2, NB])
        probs = sb("probs", [P, 2, NB, N])
        vt = sb("vt", [P, 2, NB, 2 * C])
        values = sb("values", [P, 2, NB, VW])
        col_sum = sb("col_sum", [P, NB])
        col_inv = sb("col_inv", [P, NB])
        pre = sb("pre", [P, NB, C])
        y_sb = sb("y_sb", [P, 2, N])
        stats = sb("stats", [P, 2, 2, 6])
        mean_var = sb("mean_var", [P, 2, 2])
        var_eps = sb("var_eps", [P, 2, 1])
        rstd = sb("rstd", [P, 2, 1])

        score_ps = ctx.enter_context(nc.psum_tensor("score_ps", [P, 2, N], F32))
        att_ps = ctx.enter_context(nc.psum_tensor("att_ps", [P, 2, BANK], F32))
        turn_ps = ctx.enter_context(nc.psum_tensor("turn_ps", [P, 2 * BANK], F32))

        consts_loaded = sem("consts_loaded")
        made_const = sem("made_const")
        bn_chain = sem("bn_chain")
        bn_root = sem("bn_root")
        const_mm = sem("const_mm")
        weights_ready = sem("weights_ready")
        x_loaded = [sem(f"x_loaded{i}") for i in range(XSLOTS)]
        x_hi_done = sem("x_hi_done")
        x_lo_done = sem("x_lo_done")
        q_done = sem("q_done")
        q_rounded = sem("q_rounded")
        q_split = sem("q_split")
        scores_done = sem("scores_done")
        max_done = sem("max_done")
        exp_done = sem("exp_done")
        vt_done = sem("vt_done")
        vt_copied = sem("vt_copied")
        recip_done = sem("recip_done")
        scaled_pool = sem("scaled_pool")
        scaled_dve = sem("scaled_dve")
        att_done = sem("att_done")
        col_eps_done = sem("col_eps_done")
        col_inv_done = sem("col_inv_done")
        pre_done = sem("pre_done")
        turned = sem("turned")
        relu_done = sem("relu_done")
        resid_done = sem("resid_done")
        stats_done = sem("stats_done")
        aggr_done = sem("aggr_done")
        veps_done = sem("veps_done")
        rstd_done = sem("rstd_done")
        norm_done = sem("norm_done")
        stored = [sem(f"stored{i}") for i in range(2)]

        FIRST_LOOP = 3
        TRIPS = (B - FIRST_LOOP - LOADED) // UNROLL

        class Batch:

            def __init__(self, lin, c):
                self.lin, self.c = lin, c

            def __add__(self, n):
                return Batch(self.lin, self.c + n)

            def real(self):
                return self.lin is not None or 0 <= self.c < B

            def since(self, n):
                return self.lin is not None or self.c >= n

            def count(self, per, n):
                fixed = per * self.c + n
                return fixed if self.lin is None else self.lin * (per * UNROLL) + fixed

            def index(self):
                return self.c if self.lin is None else self.lin * UNROLL + self.c

        def for_periods(eng, period):
            for s in range(-AHEAD, FIRST_LOOP):
                period(Batch(None, s))
            with eng.Fori(0, TRIPS, 1) as trip:
                for u in range(UNROLL):
                    period(Batch(trip, FIRST_LOOP + u))
            for s in range(FIRST_LOOP + TRIPS * UNROLL, B + BEHIND):
                period(Batch(None, s))

        block = ctx.enter_context(nc.Block())

        @block.sync
        def _(sp):
            for g in range(3):
                sp.dma_start(wq_rep[g * D:(g + 1) * D, :], wq).then_inc(consts_loaded, 16)
            sp.dma_start(adj_sb[:, :], adj).then_inc(consts_loaded, 16)
            for i, v in enumerate((bv, bt, gamma, beta, bn_mean, bn_var)):
                sp.dma_start(vec[:, i:i + 1], v.rearrange("(p a) -> p a", a=1)).then_inc(consts_loaded, 16)
            for b in range(XSLOTS - 2):
                sp.dma_start(x_sb[:, b, :], x[b]).then_inc(x_loaded[b], 16)

            def period(s):
                b = s + LOADED
                if b.since(XSLOTS - 2) and b.real():
                    if b.since(XSLOTS):
                        sp.wait_ge(resid_done, b.count(1, 1 - XSLOTS))
                    slot = b.c % XSLOTS
                    sp.dma_start(x_sb[:, slot, :], x[b.index()]).then_inc(x_loaded[slot], 16)
                t = s + -1
                if t.real():
                    sp.wait_ge(norm_done, t.count(1, 1))
                    sp.dma_start(out[t.index()], y_sb[:, t.c % 2, :]).then_inc(stored[t.c % 2], 16)

            for_periods(sp, period)
            for i in range(2):
                sp.wait_ge(stored[i], 16 * (B // 2))

        @block.gpsimd
        def _(pool):
            pool.memset(zeros[:, :], 0.0).then_inc(made_const, 1)
            pool.memset(minus_half[:, :], -0.5).then_inc(made_const, 1)
            pool.wait_ge(made_const, 2)
            pool.affine_select(out=ident[:, :], in_=zeros[:, :], compare_op=ALU.not_equal, fill=1.0, base=0,
                               pattern=[[-1, P]], channel_multiplier=1).then_inc(made_const, 1)
            pool.wait_ge(bn_chain, 1)
            pool.tensor_tensor(bn_inv[:, :], bn_veps[:, :], minus_half[:, :], ALU.pow).then_inc(bn_root, 1)

            def split_x(b):
                p = b.c % 2
                pool.wait_ge(x_hi_done, b.count(1, 1))
                pool.tensor_tensor(x_lo[:, p, :], x_sb[:, b.c % XSLOTS, :], x_hi[:, p, :].bitcast(F32),
                                   ALU.subtract).then_inc(x_lo_done, 1)

            def scale_values(b, g):
                p = b.c % 2
                lo, hi = RECIP_GROUPS[g]
                pool.wait_ge(recip_done, b.count(NR, g + 1))
                pool.wait_ge(vt_copied, b.count(2, 1 if hi <= NB // 2 else 2))
                pool.tensor_tensor(values[:, p, lo:hi, 0:C], vt[:, p, lo:hi, 0:C],
                                   values[:, p, lo:hi, C:C + 1].broadcast_to([P, hi - lo, C]),
                                   ALU.mult).then_inc(scaled_pool, 1)

            def add_residual(b):
                p = b.c % 2
                pool.wait_ge(relu_done, b.count(1, 1))
                pool.tensor_tensor(y_sb[:, p, :], y_sb[:, p, :], x_sb[:, b.c % XSLOTS, :],
                                   ALU.add).then_inc(resid_done, 1)

            def root(b):
                p = b.c % 2
                pool.wait_ge(veps_done, b.count(1, 1))
                pool.tensor_tensor(rstd[:, p, :], var_eps[:, p, :], minus_half[:, :],
                                   ALU.pow).then_inc(rstd_done, 1)

            def period(s):
                if (s + 2).real():
                    split_x(s + 2)
                if (s + -1).real():
                    add_residual(s + -1)
                if (s + 1).real():
                    scale_values(s + 1, 0)
                if (s + -1).real():
                    root(s + -1)
                if (s + 1).real():
                    scale_values(s + 1, 1)

            for_periods(pool, period)

        @block.scalar
        def _(act):
            act.wait_ge(const_mm, 2)
            act.copy(wq_hi[:, :], turn_ps[:, 0:REP]).then_inc(weights_ready, 1)
            act.copy(w_hi[:, C:2 * C], turn_ps[:, BANK:BANK + C]).then_inc(weights_ready, 1)
            act.wait_ge(const_mm, 4)
            act.copy(w_hi[:, 0:C], att_ps[:, 0, 0:C]).then_inc(weights_ready, 1)
            act.copy(bias_rows[0:64, :], att_ps[0:64, 1, 0:C]).then_inc(weights_ready, 1)

            def round_x(b):
                slot = b.c % XSLOTS
                act.wait_ge(x_loaded[slot], b.count(4, 16 - 4 * slot))
                act.copy(x_hi[:, b.c % 2, :], x_sb[:, slot, :]).then_inc(x_hi_done, 1)

            def round_q(b):
                p = b.c % 2
                act.wait_ge(q_done, b.count(1, 1))
                act.copy(qa[:, p, :], turn_ps[0:REP, :]).then_inc(q_rounded, 1)
                act.copy(qb[:, p, :], turn_ps[0:REP, :]).then_inc(q_rounded, 1)

            def copy_vt(b, half):
                p = b.c % 2
                if b.since(2):
                    act.wait_ge(pre_done, b.count(NO, -NO))
                act.wait_ge(vt_done, b.count(2, half + 1))
                act.copy(vt[:, p, half * 4:half * 4 + 4, :],
                         turn_ps[:, :].rearrange("p (n w) -> p n w", n=4)).then_inc(vt_copied, 1)

            def exponent(b, k):
                p = b.c % 2
                if k == 0 and b.since(2):
                    act.wait_ge(att_done, b.count(NO, -NO))
                act.wait_ge(max_done, b.count(NB, k + 1))
                act.activation(probs[:, p, k, :], score_ps[:, k % 2, :], ACT.Exp, bias=neg_max[:, p, k:k + 1],
                               accum_out=row_sum[:, p, k:k + 1]).then_inc(exp_done, 1)

            def relu(b):
                p = b.c % 2
                if b.since(2):
                    act.wait_ge(stored[p], b.count(8, -8 * p))
                act.wait_ge(turned, b.count(1, 1))
                act.activation(y_sb[:, p, :], turn_ps[:, :], ACT.Relu, bias=bn_shift[:, 0:1]).then_inc(relu_done, 1)

            def period(s):
                for k in range(NB):
                    if k == 3 and (s + 2).real():
                        round_q(s + 2)
                    if k == 5 and (s + 1).real():
                        copy_vt(s + 1, 0)
                    if k == 7 and (s + 1).real():
                        copy_vt(s + 1, 1)
                    if (s + 1).real():
                        exponent(s + 1, k)
                    if k == 0 and (s + 2).real():
                        round_x(s + 2)
                    if k == 1 and (s + -1).real():
                        relu(s + -1)

            act.wait_ge(bn_chain, 6)
            for_periods(act, period)

        @block.vector
        def _(dve):
            BV, BT, GAMMA, BETA, MEAN, VAR = range(6)
            dve.wait_ge(consts_loaded, 16 * 10)
            dve.tensor_scalar(bn_veps[:, :], vec[:, VAR:VAR + 1], EPS_BN, None, ALU.add).then_inc(bn_chain, 1)
            dve.tensor_tensor(bn_diff[:, :], vec[:, BT:BT + 1], vec[:, MEAN:MEAN + 1],
                              ALU.subtract).then_inc(bn_chain, 1)
            dve.wait_ge(bn_root, 1)
            dve.scalar_tensor_tensor(bn_scale[:, :], vec[:, GAMMA:GAMMA + 1], 0.5, bn_inv[:, :],
                                     ALU.mult, ALU.mult).then_inc(bn_chain, 1)
            dve.wait_ge(bn_chain, 3)
            dve.tensor_scalar(adj_scaled[:, :], adj_sb[:, :], bn_scale[:, 0:1], None, ALU.mult).then_inc(bn_chain, 1)
            dve.tensor_tensor(bn_part[:, :], bn_diff[:, :], bn_scale[:, :], ALU.mult).then_inc(bn_chain, 1)
            dve.wait_ge(bn_chain, 5)
            dve.scalar_tensor_tensor(bn_shift[:, :], vec[:, BETA:BETA + 1], 0.5, bn_part[:, :],
                                     ALU.mult, ALU.add).then_inc(bn_chain, 1)
            dve.wait_ge(made_const, 3)
            dve.tensor_scalar(bv_cols[:, :], zeros[:, :], vec[:, BV:BV + 1], None, ALU.add).then_inc(bn_chain, 1)
            dve.memset(bias_pick[:, :].bitcast(F32), 0.0).then_inc(bn_chain, 1)
            dve.memset(bias_rows[64:P, :].bitcast(F32), 0.0).then_inc(bn_chain, 1)
            dve.memset(values[:, :, :, C + 1:C + 2], 0.0).then_inc(bn_chain, 1)
            dve.wait_ge(bn_chain, 10)
            dve.memset(bias_pick[0:1, :].bitcast(F32), 1.0).then_inc(bn_chain, 1)
            dve.memset(bias_pick[32:33, :].bitcast(F32), 1.0).then_inc(bn_chain, 1)
            dve.wait_ge(const_mm, 2)
            dve.wait_ge(weights_ready, 2)
            dve.tensor_copy(adj_sT[:, :], turn_ps[:, BANK:BANK + C]).then_inc(bn_chain, 1)
            dve.tensor_scalar(adj_sT_neg[:, :], turn_ps[:, BANK:BANK + C], -1.0, None,
                              ALU.mult).then_inc(bn_chain, 1)
            dve.tensor_tensor(wq_lo[:, :], turn_ps[:, 0:REP], wq_hi[:, :].bitcast(F32),
                              ALU.subtract).then_inc(weights_ready, 1)
            dve.tensor_tensor(w_lo[:, C:2 * C], turn_ps[:, BANK:BANK + C], w_hi[:, C:2 * C].bitcast(F32),
                              ALU.subtract).then_inc(weights_ready, 1)
            dve.wait_ge(weights_ready, 6)
            dve.tensor_tensor(w_lo[:, 0:C], att_ps[:, 0, 0:C], w_hi[:, 0:C].bitcast(F32),
                              ALU.subtract).then_inc(weights_ready, 1)
            dve.tensor_tensor(bias_rows[32:64, :], att_ps[32:64, 1, 0:C], bias_rows[32:64, :].bitcast(F32),
                              ALU.subtract).then_inc(weights_ready, 1)

            def row_max(b, k):
                p = b.c % 2
                dve.wait_ge(scores_done, b.count(NB, k + 1))
                dve.tensor_reduce(neg_max[:, p, k:k + 1], score_ps[:, k % 2, :], AX.X, ALU.max,
                                  negate=True).then_inc(max_done, 1)

            def split_q(b):
                p = b.c % 2
                dve.wait_ge(q_rounded, b.count(2, 2))
                for t, r in ((qa, 2 * D), (qb, D)):
                    dve.tensor_tensor(t[r:r + D, p, :], turn_ps[r:r + D, :], t[r:r + D, p, :].bitcast(F32),
                                      ALU.subtract).then_inc(q_split, 1)

            def row_recip(b, g):
                p = b.c % 2
                lo, hi = RECIP_GROUPS[g]
                dve.wait_ge(exp_done, b.count(NB, hi))
                dve.reciprocal(values[:, p, lo:hi, C:C + 1], row_sum[:, p, lo:hi]).then_inc(recip_done, 1)

            def scale_last_values(b):
                p = b.c % 2
                lo, hi = RECIP_GROUPS[2]
                dve.wait_ge(recip_done, b.count(NR, NR))
                dve.wait_ge(vt_copied, b.count(2, 2))
                dve.tensor_tensor(values[:, p, lo:hi, 0:C], vt[:, p, lo:hi, 0:C],
                                  values[:, p, lo:hi, C:C + 1].broadcast_to([P, hi - lo, C]),
                                  ALU.mult).then_inc(scaled_dve, 1)

            def combine(b, g):
                p = b.c % 2
                bank = (b.c * NO + g) % 2
                lo, hi = OUT_GROUPS[g]
                n = hi - lo
                att = att_ps[:, bank, 0:n * VW].rearrange("p (j w) -> p j w", w=VW)
                dve.wait_ge(att_done, b.count(NO, g + 1))
                dve.tensor_scalar(col_sum[:, lo:hi], att[:, :, C], EPS_COL, None, ALU.add).then_inc(col_eps_done, 1)
                dve.wait_ge(col_eps_done, b.count(NO, g + 1))
                dve.reciprocal(col_inv[:, lo:hi], col_sum[:, lo:hi]).then_inc(col_inv_done, 1)
                dve.wait_ge(col_inv_done, b.count(NO, g + 1))
                if g == 0 and b.since(1):
                    dve.wait_ge(turned, b.count(1, 0))
                for j in range(lo, hi):
                    last = dve.scalar_tensor_tensor(pre[:, j, :], att[:, j - lo, 0:C], col_inv[:, j:j + 1],
                                                    vt[:, p, j, C:2 * C], ALU.mult, ALU.add)
                last.then_inc(pre_done, 1)

            def statistics(b):
                p = b.c % 2
                dve.wait_ge(resid_done, b.count(1, 1))
                for h in range(2):
                    dve.bn_stats(stats[:, p, h, :], y_sb[:, p, h * BANK:(h + 1) * BANK]).then_inc(stats_done, 1)

            def aggregate(b):
                p = b.c % 2
                dve.bn_aggr(mean_var[:, p, :], stats[:, p, :, :]).then_inc(aggr_done, 1)
                dve.wait_ge(aggr_done, b.count(1, 1))
                dve.tensor_scalar(var_eps[:, p, :], mean_var[:, p, 1:2], EPS_LN / 4, None,
                                  ALU.add).then_inc(veps_done, 1)

            def normalise(b):
                p = b.c % 2
                dve.wait_ge(rstd_done, b.count(1, 1))
                dve.tensor_scalar(y_sb[:, p, :], y_sb[:, p, :], mean_var[:, p, 0:1], rstd[:, p, 0:1],
                                  ALU.subtract, ALU.mult).then_inc(norm_done, 1)

            def period(s):
                for k in range(NB):
                    if k == 5 and (s + -1).real():
                        dve.wait_ge(stats_done, (s + -1).count(2, 2))
                    if (s + 1).real():
                        row_max(s + 1, k)
                    if k == 5 and (s + -1).real():
                        aggregate(s + -1)
                    if k == 0 and s.real():
                        row_recip(s, 2)
                        scale_last_values(s)
                    if k == 0 and (s + -1).real():
                        combine(s + -1, 2)
                    if k == 3 and (s + 2).real():
                        split_q(s + 2)
                    if k == 3 and s.real():
                        combine(s, 0)
                    if k == 4 and (s + 1).real():
                        row_recip(s + 1, 0)
                    if k == 4 and (s + -1).real():
                        statistics(s + -1)
                    if k == 6 and s.real():
                        combine(s, 1)
                    if k == 6 and (s + 1).real():
                        row_recip(s + 1, 1)
                    if k == 6 and (s + -1).real():
                        normalise(s + -1)

            for_periods(dve, period)

        @block.tensor
        def _(pe):
            pe.wait_ge(consts_loaded, 16 * 10)
            pe.wait_ge(made_const, 3)
            pe.transpose(turn_ps[:, 0:REP], wq_rep[:, :], ident[0:REP, 0:REP]).then_inc(const_mm, 1)
            pe.wait_ge(bn_chain, 4)
            pe.transpose(turn_ps[:, BANK:BANK + C], adj_scaled[:, :], ident[:, :]).then_inc(const_mm, 1)
            pe.wait_ge(bn_chain, 14)
            pe.matmul(att_ps[:, 0, 0:C], adj_sb[:, :], adj_sT_neg[:, :], start=True, stop=True).then_inc(const_mm, 1)
            pe.matmul(att_ps[:, 1, 0:C], bv_cols[:, :], adj_sT_neg[:, :], start=True, stop=True).then_inc(const_mm, 1)
            pe.wait_ge(weights_ready, 8)

            def project(b):
                p = b.c % 2
                if b.since(3):
                    pe.wait_ge(relu_done, b.count(1, -2))
                pe.wait_ge(x_lo_done, b.count(1, 1))
                for h in range(2):
                    cols = slice(h * BANK, (h + 1) * BANK)
                    o = turn_ps[0:REP, cols]
                    pe.matmul(o, wq_hi[:, :], x_hi[:, p, cols], start=True, stop=False)
                    pe.matmul(o, wq_hi[:, :], x_lo[:, p, cols], start=False, stop=False)
                    last = pe.matmul(o, wq_lo[:, :], x_hi[:, p, cols], start=False, stop=True)
                last.then_inc(q_done, 1)

            def scores(b, k):
                p = b.c % 2
                if k == 0:
                    pe.wait_ge(q_split, b.count(2, 2))
                if k >= 2 or b.since(1):
                    pe.wait_ge(exp_done, b.count(NB, k - 1))
                for h in range(2):
                    cols = slice(h * BANK, (h + 1) * BANK)
                    last = pe.matmul(score_ps[:, k % 2, cols], qa[:, p, k * P:(k + 1) * P], qb[:, p, cols],
                                     start=True, stop=True)
                last.then_inc(scores_done, 1)

            def values_and_adj(b, half):
                p = b.c % 2
                if half == 0:
                    if (b + 1).real():
                        pe.wait_ge(q_split, b.count(2, 4))
                    else:
                        pe.wait_ge(relu_done, b.count(1, -1))
                else:
                    pe.wait_ge(vt_copied, b.count(2, 1))
                for i in range(4):
                    rows = slice((4 * half + i) * P, (4 * half + i + 1) * P)
                    o = turn_ps[:, i * 2 * C:(i + 1) * 2 * C]
                    pe.matmul(o, x_hi[:, p, rows], w_hi[:, :], start=True, stop=False)
                    pe.matmul(o, x_hi[:, p, rows], w_lo[:, :], start=False, stop=False)
                    pe.matmul(o[:, 0:C], bias_pick[:, :], bias_rows[:, :], start=False, stop=False,
                              skip_group_check=True)
                    last = pe.matmul(o, x_lo[:, p, rows], w_hi[:, :], start=False, stop=True)
                last.then_inc(vt_done, 1)

            def attend(b, j):
                p = b.c % 2
                g = [n for n, (lo, hi) in enumerate(OUT_GROUPS) if lo <= j < hi][0]
                lo, hi = OUT_GROUPS[g]
                bank = (b.c * NO + g) % 2
                o = att_ps[:, bank, (j - lo) * VW:(j - lo + 1) * VW]
                if j == lo and (g >= 2 or b.since(1)):
                    pe.wait_ge(pre_done, b.count(NO, g - 1))
                for i in range(NB):
                    if j == 0 and i == RECIP_GROUPS[0][0]:
                        pe.wait_ge(scaled_pool, b.count(2, 1))
                    if j == 0 and i == RECIP_GROUPS[1][0]:
                        pe.wait_ge(scaled_pool, b.count(2, 2))
                    if j == 0 and i == RECIP_GROUPS[2][0]:
                        pe.wait_ge(scaled_dve, b.count(1, 1))
                    last = pe.matmul(o, probs[:, p, i, j * P:(j + 1) * P], values[:, p, i, :],
                                     start=(i == 0), stop=(i == NB - 1))
                if j == hi - 1:
                    last.then_inc(att_done, 1)

            def turn(b):
                pe.wait_ge(vt_copied, (b + 1).count(2, 2) if (b + 1).real() else b.count(2, 2))
                pe.wait_ge(pre_done, b.count(NO, NO))
                for j in range(NB):
                    last = pe.transpose(turn_ps[:, j * P:(j + 1) * P], pre[:, j, :], ident[:, :])
                last.then_inc(turned, 1)

            def period(s):
                for k in range(NB):
                    if (s + 1).real():
                        scores(s + 1, k)
                    if k == 1 and (s + -1).real():
                        turn(s + -1)
                    if s.real():
                        attend(s, k)
                    if k == 2 and (s + 2).real():
                        project(s + 2)
                    if k == 4 and (s + 1).real():
                        values_and_adj(s + 1, 0)
                    if k == 6 and (s + 1).real():
                        values_and_adj(s + 1, 1)

            for_periods(pe, period)


_INS = ['x', 'adj', 'L0_gnn_wq', 'L0_gnn_bv', 'L0_gnn_bt', 'L0_gnn_gamma', 'L0_gnn_beta',
        'L0_gnn_bn_mean', 'L0_gnn_bn_var']


def kernel(**inputs):
    import numpy as _np
    import concourse.bacc as _bacc
    from concourse import mybir as _mybir
    from concourse.bass_utils import run_bass_kernel_spmd as _run

    nc = _bacc.Bacc("TRN2", target_bir_lowering=False, num_devices=1)
    arrays, args = {}, []
    for name in _INS:
        a = _np.ascontiguousarray(inputs[name])
        arrays[f"in_{name}_dram"] = a
        args.append(nc.dram_tensor(f"in_{name}_dram", a.shape, _mybir.dt.from_np(a.dtype), kind="ExternalInput").ap())
    shape = inputs['x'].shape
    args.append(nc.dram_tensor("out_0_dram", shape, _mybir.dt.from_np(_np.dtype('float32')),
                               kind="ExternalOutput").ap())
    attention_kernel(nc, *args)
    r = _run(nc, [arrays], core_ids=[0])
    return r.results[0]["out_0_dram"]
```

```python
from contextlib import ExitStack

import concourse.bass as bass
from concourse import mybir

F32 = mybir.dt.float32
F32R = mybir.dt.float32r
ALU = mybir.AluOpType
ACT = mybir.ActivationFunctionType
AX = mybir.AxisListType

P = 128
BANK = 512
EPS_COL = 1e-9
EPS_BN = 1e-5
EPS_LN = 1e-5
XSLOTS = 4
UNROLL = 4
BEHIND, AHEAD, LOADED = 2, 2, 3


def attention_kernel(nc, x, adj, wq, bv, bt, gamma, beta, bn_mean, bn_var, out):
    B, C, N = x.shape
    D = wq.shape[0]
    NB = N // P
    REP = 3 * D
    VW = C + 1
    AW = C + 2
    RECIP_GROUPS = [(0, 4), (4, 6), (6, 8)]
    OUT_GROUPS = [(0, 3), (3, 6), (6, 8)]
    NR, NO = len(RECIP_GROUPS), len(OUT_GROUPS)
    assert C == P and N == 2 * BANK and NB == 8 and B % UNROLL == 0 and REP <= P

    with ExitStack() as ctx:
        def sb(name, shape, dt=F32):
            return ctx.enter_context(nc.sbuf_tensor(name, shape, dt))

        def sem(name):
            return ctx.enter_context(nc.semaphore(name))

        adj_sb = sb("adj_sb", [P, C])
        wq_rep = sb("wq_rep", [REP, C])
        vec = sb("vec", [P, 6])
        zeros = sb("zeros", [P, P])
        ident = sb("ident", [P, P])
        minus_half = sb("minus_half", [P, 1])
        bn_veps = sb("bn_veps", [P, 1])
        bn_inv = sb("bn_inv", [P, 1])
        bn_scale = sb("bn_scale", [P, 1])
        bn_diff = sb("bn_diff", [P, 1])
        bn_part = sb("bn_part", [P, 1])
        bn_shift = sb("bn_shift", [P, 1])
        adj_scaled = sb("adj_scaled", [P, C])
        adj_sT = sb("adj_sT", [P, C])
        adj_sT_neg = sb("adj_sT_neg", [P, C])
        bv_cols = sb("bv_cols", [P, P])
        wq_hi = sb("wq_hi", [P, REP], F32R)
        wq_lo = sb("wq_lo", [P, REP], F32R)
        w_hi = sb("w_hi", [P, 2 * C], F32R)
        w_lo = sb("w_lo", [P, 2 * C], F32R)
        value_bias = sb("value_bias", [P, C])

        x_sb = sb("x_sb", [P, XSLOTS, N])
        x_hi = sb("x_hi", [P, 2, N], F32R)
        x_lo = sb("x_lo", [P, 2, N], F32R)
        qa = sb("qa", [REP, 2, N], F32R)
        qb = sb("qb", [REP, 2, N], F32R)
        neg_max = sb("neg_max", [P, 2, NB])
        row_sum = sb("row_sum", [P, 2, NB])
        probs = sb("probs", [P, 2, NB, N])
        vt = sb("vt", [P, 2, NB, 2 * C])
        values = sb("values", [P, 2, NB, VW])
        col_sum = sb("col_sum", [P, NB])
        col_inv = sb("col_inv", [P, NB])
        pre = sb("pre", [P, NB, C])
        y_sb = sb("y_sb", [P, 2, N])
        stats = sb("stats", [P, 2, 2, 6])
        mean_var = sb("mean_var", [P, 2, 2])
        var_eps = sb("var_eps", [P, 2, 1])
        rstd = sb("rstd", [P, 2, 1])

        score_ps = ctx.enter_context(nc.psum_tensor("score_ps", [P, 2, N], F32))
        att_ps = ctx.enter_context(nc.psum_tensor("att_ps", [P, 2, BANK], F32))
        turn_ps = ctx.enter_context(nc.psum_tensor("turn_ps", [P, 2 * BANK], F32))

        consts_loaded = sem("consts_loaded")
        made_const = sem("made_const")
        bn_chain = sem("bn_chain")
        bn_root = sem("bn_root")
        const_mm = sem("const_mm")
        weights_ready = sem("weights_ready")
        x_loaded = [sem(f"x_loaded{i}") for i in range(XSLOTS)]
        x_hi_done = sem("x_hi_done")
        x_lo_done = sem("x_lo_done")
        q_done = sem("q_done")
        q_rounded = sem("q_rounded")
        q_split = sem("q_split")
        scores_done = sem("scores_done")
        max_done = sem("max_done")
        exp_done = sem("exp_done")
        vt_done = sem("vt_done")
        vt_copied = sem("vt_copied")
        vt_biased = sem("vt_biased")
        recip_done = sem("recip_done")
        scaled_pool = sem("scaled_pool")
        scaled_dve = sem("scaled_dve")
        att_done = sem("att_done")
        col_eps_done = sem("col_eps_done")
        col_inv_done = sem("col_inv_done")
        pre_done = sem("pre_done")
        turned = sem("turned")
        relu_done = sem("relu_done")
        resid_done = sem("resid_done")
        stats_done = sem("stats_done")
        aggr_done = sem("aggr_done")
        veps_done = sem("veps_done")
        rstd_done = sem("rstd_done")
        norm_done = sem("norm_done")
        stored = [sem(f"stored{i}") for i in range(2)]

        FIRST_LOOP = 4
        TRIPS = (B - FIRST_LOOP - LOADED) // UNROLL

        PRELUDE = 2

        class Batch:

            def __init__(self, lin, c):
                self.lin, self.c = lin, c

            def __add__(self, n):
                return Batch(self.lin, self.c + n)

            def real(self):
                return self.lin is not None or 0 <= self.c < B

            def since(self, n):
                return self.lin is not None or self.c >= n

            def count(self, per, n):
                fixed = per * self.c + n
                return fixed if self.lin is None else self.lin * (per * UNROLL) + fixed

            def index(self):
                return self.c if self.lin is None else self.lin * UNROLL + self.c

        def for_periods(eng, period):
            for s in range(-AHEAD, FIRST_LOOP):
                period(Batch(None, s))
            with eng.Fori(0, TRIPS, 1) as trip:
                for u in range(UNROLL):
                    period(Batch(trip, FIRST_LOOP + u))
            for s in range(FIRST_LOOP + TRIPS * UNROLL, B + BEHIND):
                period(Batch(None, s))

        block = ctx.enter_context(nc.Block())

        @block.sync
        def _(sp):
            sp.dma_start(x_sb[:, 0, :], x[0]).then_inc(x_loaded[0], 16)
            for g in range(3):
                sp.dma_start(wq_rep[g * D:(g + 1) * D, :], wq).then_inc(consts_loaded, 16)
            sp.dma_start(adj_sb[:, :], adj).then_inc(consts_loaded, 16)
            for i, v in enumerate((bv, bt, gamma, beta, bn_mean, bn_var)):
                sp.dma_start(vec[:, i:i + 1], v.rearrange("(p a) -> p a", a=1)).then_inc(consts_loaded, 16)
            for b in range(1, PRELUDE):
                sp.dma_start(x_sb[:, b, :], x[b]).then_inc(x_loaded[b], 16)

            def period(s):
                b = s + LOADED
                if b.since(PRELUDE) and b.real():
                    if b.since(XSLOTS):
                        sp.wait_ge(resid_done, b.count(1, 1 - XSLOTS))
                    slot = b.c % XSLOTS
                    sp.dma_start(x_sb[:, slot, :], x[b.index()]).then_inc(x_loaded[slot], 16)
                t = s + -BEHIND
                if t.real():
                    sp.wait_ge(norm_done, t.count(1, 1))
                    sp.dma_start(out[t.index()], y_sb[:, t.c % 2, :]).then_inc(stored[t.c % 2], 16)

            for_periods(sp, period)
            for i in range(2):
                sp.wait_ge(stored[i], 16 * (B // 2))

        @block.gpsimd
        def _(pool):
            pool.memset(zeros[:, :], 0.0).then_inc(made_const, 1)
            pool.memset(minus_half[:, :], -0.5).then_inc(made_const, 1)
            pool.wait_ge(made_const, 2)
            pool.affine_select(out=ident[:, :], in_=zeros[:, :], compare_op=ALU.not_equal, fill=1.0, base=0,
                               pattern=[[-1, P]], channel_multiplier=1).then_inc(made_const, 1)
            pool.wait_ge(bn_chain, 1)
            pool.tensor_tensor(bn_inv[:, :], bn_veps[:, :], minus_half[:, :], ALU.pow).then_inc(bn_root, 1)

            def split_x(b):
                p = b.c % 2
                pool.wait_ge(x_hi_done, b.count(1, 1))
                pool.tensor_tensor(x_lo[:, p, :], x_sb[:, b.c % XSLOTS, :], x_hi[:, p, :].bitcast(F32),
                                   ALU.subtract).then_inc(x_lo_done, 1)

            def add_bias(b, half):
                v = vt[:, b.c % 2, 4 * half:4 * half + 4, 0:C]
                pool.wait_ge(vt_copied, b.count(2, half + 1))
                pool.tensor_tensor(v, v, value_bias[:, None, :].broadcast_to([P, 4, C]),
                                   ALU.add).then_inc(vt_biased, 1)

            def scale_values(b, g):
                p = b.c % 2
                lo, hi = RECIP_GROUPS[g]
                pool.wait_ge(recip_done, b.count(NR, g + 1))
                pool.wait_ge(vt_biased, b.count(2, 1 if hi <= NB // 2 else 2))
                pool.tensor_tensor(values[:, p, lo:hi, 0:C], vt[:, p, lo:hi, 0:C],
                                   values[:, p, lo:hi, C:C + 1].broadcast_to([P, hi - lo, C]),
                                   ALU.mult).then_inc(scaled_pool, 1)

            def add_residual(b):
                p = b.c % 2
                pool.wait_ge(relu_done, b.count(1, 1))
                pool.tensor_tensor(y_sb[:, p, :], y_sb[:, p, :], x_sb[:, b.c % XSLOTS, :],
                                   ALU.add).then_inc(resid_done, 1)

            def root(b):
                p = b.c % 2
                pool.wait_ge(veps_done, b.count(1, 1))
                pool.tensor_tensor(rstd[:, p, :], var_eps[:, p, :], minus_half[:, :],
                                   ALU.pow).then_inc(rstd_done, 1)

            def period(s):
                if (s + 1).real():
                    add_bias(s + 1, 0)
                    add_bias(s + 1, 1)
                if (s + 2).real() and (s + 2).since(PRELUDE):
                    split_x(s + 2)
                if (s + -1).real():
                    add_residual(s + -1)
                if (s + 1).real():
                    scale_values(s + 1, 0)
                if (s + -2).real():
                    root(s + -2)
                if (s + 1).real():
                    scale_values(s + 1, 1)

            for b in range(PRELUDE):
                split_x(Batch(None, b))
            for_periods(pool, period)

        @block.scalar
        def _(act):
            def round_x(b):
                slot = b.c % XSLOTS
                act.wait_ge(x_loaded[slot], b.count(4, 16 - 4 * slot))
                act.copy(x_hi[:, b.c % 2, :], x_sb[:, slot, :]).then_inc(x_hi_done, 1)

            round_x(Batch(None, 0))
            act.wait_ge(const_mm, 2)
            act.copy(wq_hi[:, :], turn_ps[:, 0:REP]).then_inc(weights_ready, 1)
            act.copy(w_hi[:, C:2 * C], turn_ps[:, BANK:BANK + C]).then_inc(weights_ready, 1)
            act.wait_ge(const_mm, 4)
            act.copy(w_hi[:, 0:C], att_ps[:, 0, 0:C]).then_inc(weights_ready, 1)
            act.copy(value_bias[:, :], att_ps[:, 1, 0:C]).then_inc(weights_ready, 1)
            for b in range(1, PRELUDE):
                round_x(Batch(None, b))

            def round_q(b):
                p = b.c % 2
                act.wait_ge(q_done, b.count(1, 1))
                act.copy(qa[:, p, :], turn_ps[0:REP, :]).then_inc(q_rounded, 1)
                act.copy(qb[:, p, :], turn_ps[0:REP, :]).then_inc(q_rounded, 1)

            def copy_vt(b, half):
                p = b.c % 2
                if b.since(2):
                    act.wait_ge(pre_done, b.count(NO, -NO))
                act.wait_ge(vt_done, b.count(2, half + 1))
                act.copy(vt[:, p, half * 4:half * 4 + 4, :],
                         turn_ps[:, :].rearrange("p (n w) -> p n w", n=4)).then_inc(vt_copied, 1)

            def exponent(b, k):
                p = b.c % 2
                if k == 0 and b.since(2):
                    act.wait_ge(att_done, b.count(NO, -NO))
                act.wait_ge(max_done, b.count(NB, k + 1))
                act.activation(probs[:, p, k, :], score_ps[:, k % 2, :], ACT.Exp, bias=neg_max[:, p, k:k + 1],
                               accum_out=row_sum[:, p, k:k + 1]).then_inc(exp_done, 1)

            def relu(b):
                p = b.c % 2
                if b.since(2):
                    act.wait_ge(stored[p], b.count(8, -8 * p))
                act.wait_ge(turned, b.count(1, 1))
                act.activation(y_sb[:, p, :], turn_ps[:, :], ACT.Relu, bias=bn_shift[:, 0:1]).then_inc(relu_done, 1)

            def period(s):
                for k in range(NB):
                    if k == 4 and (s + 2).real():
                        round_q(s + 2)
                    if (s + 1).real():
                        exponent(s + 1, k)
                    if k == 0 and (s + 1).real():
                        copy_vt(s + 1, 0)
                    if k == 0 and (s + 2).real() and (s + 2).since(PRELUDE):
                        round_x(s + 2)
                    if k == 1 and (s + 1).real():
                        copy_vt(s + 1, 1)
                    if k == 2 and (s + -1).real():
                        relu(s + -1)

            act.wait_ge(bn_chain, 6)
            for_periods(act, period)

        @block.vector
        def _(dve):
            BV, BT, GAMMA, BETA, MEAN, VAR = range(6)
            dve.wait_ge(consts_loaded, 16 * 10)
            dve.tensor_scalar(bn_veps[:, :], vec[:, VAR:VAR + 1], EPS_BN, None, ALU.add).then_inc(bn_chain, 1)
            dve.tensor_tensor(bn_diff[:, :], vec[:, BT:BT + 1], vec[:, MEAN:MEAN + 1],
                              ALU.subtract).then_inc(bn_chain, 1)
            dve.wait_ge(bn_root, 1)
            dve.scalar_tensor_tensor(bn_scale[:, :], vec[:, GAMMA:GAMMA + 1], 0.5, bn_inv[:, :],
                                     ALU.mult, ALU.mult).then_inc(bn_chain, 1)
            dve.wait_ge(bn_chain, 3)
            dve.tensor_scalar(adj_scaled[:, :], adj_sb[:, :], bn_scale[:, 0:1], None, ALU.mult).then_inc(bn_chain, 1)
            dve.tensor_tensor(bn_part[:, :], bn_diff[:, :], bn_scale[:, :], ALU.mult).then_inc(bn_chain, 1)
            dve.wait_ge(bn_chain, 5)
            dve.scalar_tensor_tensor(bn_shift[:, :], vec[:, BETA:BETA + 1], 0.5, bn_part[:, :],
                                     ALU.mult, ALU.add).then_inc(bn_chain, 1)
            dve.wait_ge(made_const, 3)
            dve.tensor_scalar(bv_cols[:, :], zeros[:, :], vec[:, BV:BV + 1], None, ALU.add).then_inc(bn_chain, 1)
            dve.wait_ge(const_mm, 2)
            dve.wait_ge(weights_ready, 2)
            dve.tensor_copy(adj_sT[:, :], turn_ps[:, BANK:BANK + C]).then_inc(bn_chain, 1)
            dve.tensor_scalar(adj_sT_neg[:, :], turn_ps[:, BANK:BANK + C], -1.0, None,
                              ALU.mult).then_inc(bn_chain, 1)
            dve.tensor_tensor(wq_lo[:, :], turn_ps[:, 0:REP], wq_hi[:, :].bitcast(F32),
                              ALU.subtract).then_inc(weights_ready, 1)
            dve.tensor_tensor(w_lo[:, C:2 * C], turn_ps[:, BANK:BANK + C], w_hi[:, C:2 * C].bitcast(F32),
                              ALU.subtract).then_inc(weights_ready, 1)
            dve.wait_ge(weights_ready, 6)
            dve.tensor_tensor(w_lo[:, 0:C], att_ps[:, 0, 0:C], w_hi[:, 0:C].bitcast(F32),
                              ALU.subtract).then_inc(weights_ready, 1)

            def row_max(b, k):
                p = b.c % 2
                dve.wait_ge(scores_done, b.count(NB, k + 1))
                dve.tensor_reduce(neg_max[:, p, k:k + 1], score_ps[:, k % 2, :], AX.X, ALU.max,
                                  negate=True).then_inc(max_done, 1)

            def split_q(b, part):
                p = b.c % 2
                t, r = ((qa, 2 * D), (qb, D))[part]
                dve.wait_ge(q_rounded, b.count(2, 2))
                dve.tensor_tensor(t[r:r + D, p, :], turn_ps[r:r + D, :], t[r:r + D, p, :].bitcast(F32),
                                  ALU.subtract).then_inc(q_split, 1)

            def row_recip(b, g):
                p = b.c % 2
                lo, hi = RECIP_GROUPS[g]
                dve.wait_ge(exp_done, b.count(NB, hi))
                dve.reciprocal(values[:, p, lo:hi, C:C + 1], row_sum[:, p, lo:hi]).then_inc(recip_done, 1)

            def scale_last_values(b):
                p = b.c % 2
                lo, hi = RECIP_GROUPS[2]
                dve.wait_ge(recip_done, b.count(NR, NR))
                dve.wait_ge(vt_biased, b.count(2, 2))
                dve.tensor_tensor(values[:, p, lo:hi, 0:C], vt[:, p, lo:hi, 0:C],
                                  values[:, p, lo:hi, C:C + 1].broadcast_to([P, hi - lo, C]),
                                  ALU.mult).then_inc(scaled_dve, 1)

            def combine(b, g):
                p = b.c % 2
                bank = (b.c * NO + g) % 2
                lo, hi = OUT_GROUPS[g]
                n = hi - lo
                att = att_ps[:, bank, 0:n * AW].rearrange("p (j w) -> p j w", w=AW)
                dve.wait_ge(att_done, b.count(NO, g + 1))
                dve.tensor_scalar(col_sum[:, lo:hi], att[:, :, C], EPS_COL, None, ALU.add).then_inc(col_eps_done, 1)
                dve.wait_ge(col_eps_done, b.count(NO, g + 1))
                dve.reciprocal(col_inv[:, lo:hi], col_sum[:, lo:hi]).then_inc(col_inv_done, 1)
                dve.wait_ge(col_inv_done, b.count(NO, g + 1))
                if g == 0 and b.since(1):
                    dve.wait_ge(turned, b.count(1, 0))
                for j in range(lo, hi):
                    last = dve.scalar_tensor_tensor(pre[:, j, :], att[:, j - lo, 0:C], col_inv[:, j:j + 1],
                                                    vt[:, p, j, C:2 * C], ALU.mult, ALU.add)
                last.then_inc(pre_done, 1)

            def statistics(b):
                p = b.c % 2
                dve.wait_ge(resid_done, b.count(1, 1))
                for h in range(2):
                    dve.bn_stats(stats[:, p, h, :], y_sb[:, p, h * BANK:(h + 1) * BANK]).then_inc(stats_done, 1)

            def aggregate(b):
                p = b.c % 2
                dve.bn_aggr(mean_var[:, p, :], stats[:, p, :, :]).then_inc(aggr_done, 1)
                dve.wait_ge(aggr_done, b.count(1, 1))
                dve.tensor_scalar(var_eps[:, p, :], mean_var[:, p, 1:2], EPS_LN / 4, None,
                                  ALU.add).then_inc(veps_done, 1)

            def normalise(b):
                p = b.c % 2
                dve.wait_ge(rstd_done, b.count(1, 1))
                dve.tensor_scalar(y_sb[:, p, :], y_sb[:, p, :], mean_var[:, p, 0:1], rstd[:, p, 0:1],
                                  ALU.subtract, ALU.mult).then_inc(norm_done, 1)

            def period(s):
                for k in range(NB):
                    if k == 2 and (s + -2).real():
                        dve.wait_ge(stats_done, (s + -2).count(2, 2))
                    if (s + 1).real():
                        row_max(s + 1, k)
                    if k == 0 and (s + -1).real():
                        combine(s + -1, 2)
                    if k == 1 and (s + -2).real():
                        statistics(s + -2)
                    if k == 2 and (s + -2).real():
                        aggregate(s + -2)
                    if k == 3 and s.real():
                        combine(s, 0)
                    if k == 4 and (s + 1).real():
                        row_recip(s + 1, 0)
                    if k in (4, 5) and (s + 2).real():
                        split_q(s + 2, k - 4)
                    if k == 6 and s.real():
                        combine(s, 1)
                    if k == 6 and (s + 1).real():
                        row_recip(s + 1, 1)
                    if k == 7 and (s + -2).real():
                        normalise(s + -2)
                    if k == 7 and (s + 1).real():
                        row_recip(s + 1, 2)
                        scale_last_values(s + 1)

            for_periods(dve, period)

        @block.tensor
        def _(pe):
            pe.wait_ge(consts_loaded, 16 * 10)
            pe.wait_ge(made_const, 3)
            pe.transpose(turn_ps[:, 0:REP], wq_rep[:, :], ident[0:REP, 0:REP]).then_inc(const_mm, 1)
            pe.wait_ge(bn_chain, 4)
            pe.transpose(turn_ps[:, BANK:BANK + C], adj_scaled[:, :], ident[:, :]).then_inc(const_mm, 1)
            pe.wait_ge(bn_chain, 9)
            pe.matmul(att_ps[:, 0, 0:C], adj_sb[:, :], adj_sT_neg[:, :], start=True, stop=True).then_inc(const_mm, 1)
            pe.matmul(att_ps[:, 1, 0:C], bv_cols[:, :], adj_sT_neg[:, :], start=True, stop=True).then_inc(const_mm, 1)
            pe.wait_ge(weights_ready, 7)

            def project(b):
                p = b.c % 2
                if b.since(3):
                    pe.wait_ge(relu_done, b.count(1, -2))
                elif b.since(1):
                    pe.wait_ge(vt_copied, b.count(2, 0))
                pe.wait_ge(x_lo_done, b.count(1, 1))
                for h in range(2):
                    cols = slice(h * BANK, (h + 1) * BANK)
                    o = turn_ps[0:REP, cols]
                    pe.matmul(o, wq_hi[:, :], x_hi[:, p, cols], start=True, stop=False)
                    pe.matmul(o, wq_hi[:, :], x_lo[:, p, cols], start=False, stop=False)
                    last = pe.matmul(o, wq_lo[:, :], x_hi[:, p, cols], start=False, stop=True)
                last.then_inc(q_done, 1)

            def scores(b, k):
                p = b.c % 2
                if k == 0:
                    pe.wait_ge(q_split, b.count(2, 2))
                if k >= 2 or b.since(1):
                    pe.wait_ge(exp_done, b.count(NB, k - 1))
                for h in range(2):
                    cols = slice(h * BANK, (h + 1) * BANK)
                    last = pe.matmul(score_ps[:, k % 2, cols], qa[:, p, k * P:(k + 1) * P], qb[:, p, cols],
                                     start=True, stop=True)
                last.then_inc(scores_done, 1)

            def values_and_adj(b, half):
                p = b.c % 2
                if half == 0:
                    pe.wait_ge(q_split, b.count(2, 2))
                else:
                    pe.wait_ge(vt_copied, b.count(2, 1))
                for i in range(4):
                    rows = slice((4 * half + i) * P, (4 * half + i + 1) * P)
                    o = turn_ps[:, i * 2 * C:(i + 1) * 2 * C]
                    pe.matmul(o, x_hi[:, p, rows], w_hi[:, :], start=True, stop=False)
                    pe.matmul(o, x_hi[:, p, rows], w_lo[:, :], start=False, stop=False)
                    last = pe.matmul(o, x_lo[:, p, rows], w_hi[:, :], start=False, stop=True)
                last.then_inc(vt_done, 1)

            def attend(b, j):
                p = b.c % 2
                g = [n for n, (lo, hi) in enumerate(OUT_GROUPS) if lo <= j < hi][0]
                lo, hi = OUT_GROUPS[g]
                bank = (b.c * NO + g) % 2
                o = att_ps[:, bank, (j - lo) * AW:(j - lo) * AW + VW]
                if j == lo and (g >= 2 or b.since(1)):
                    pe.wait_ge(pre_done, b.count(NO, g - 1))
                for i in range(NB):
                    if j == 0 and i == RECIP_GROUPS[0][0]:
                        pe.wait_ge(scaled_pool, b.count(2, 1))
                    if j == 0 and i == RECIP_GROUPS[1][0]:
                        pe.wait_ge(scaled_pool, b.count(2, 2))
                    if j == 0 and i == RECIP_GROUPS[2][0]:
                        pe.wait_ge(scaled_dve, b.count(1, 1))
                    last = pe.matmul(o, probs[:, p, i, j * P:(j + 1) * P], values[:, p, i, :],
                                     start=(i == 0), stop=(i == NB - 1))
                if j == hi - 1:
                    last.then_inc(att_done, 1)

            def turn(b):
                pe.wait_ge(vt_copied, (b + 2).count(2, 2) if (b + 2).real() else (b + 1).count(2, 2)
                           if (b + 1).real() else b.count(2, 2))
                pe.wait_ge(pre_done, b.count(NO, NO))
                for j in range(NB):
                    last = pe.transpose(turn_ps[:, j * P:(j + 1) * P], pre[:, j, :], ident[:, :])
                last.then_inc(turned, 1)

            def period(s):
                for k in range(NB):
                    if (s + 1).real():
                        scores(s + 1, k)
                    if k == 0 and (s + 1).real():
                        values_and_adj(s + 1, 0)
                    if s.real():
                        attend(s, k)
                    if k == 3 and (s + 2).real():
                        project(s + 2)
                    if k == 1 and (s + 1).real():
                        values_and_adj(s + 1, 1)
                    if k == 2 and (s + -1).real():
                        turn(s + -1)

            for_periods(pe, period)


_INS = ['x', 'adj', 'L0_gnn_wq', 'L0_gnn_bv', 'L0_gnn_bt', 'L0_gnn_gamma', 'L0_gnn_beta',
        'L0_gnn_bn_mean', 'L0_gnn_bn_var']


def kernel(**inputs):
    import numpy as _np
    import concourse.bacc as _bacc
    from concourse import mybir as _mybir
    from concourse.bass_utils import run_bass_kernel_spmd as _run

    nc = _bacc.Bacc("TRN2", target_bir_lowering=False, num_devices=1)
    arrays, args = {}, []
    for name in _INS:
        a = _np.ascontiguousarray(inputs[name])
        arrays[f"in_{name}_dram"] = a
        args.append(nc.dram_tensor(f"in_{name}_dram", a.shape, _mybir.dt.from_np(a.dtype), kind="ExternalInput").ap())
    shape = inputs['x'].shape
    args.append(nc.dram_tensor("out_0_dram", shape, _mybir.dt.from_np(_np.dtype('float32')),
                               kind="ExternalOutput").ap())
    attention_kernel(nc, *args)
    r = _run(nc, [arrays], core_ids=[0])
    return r.results[0]["out_0_dram"]
```
